# Optimizing a Trainium2 kernel written in Bass

```python
import numpy as np
import jax
import jax.numpy as jnp

def _softmax(x, axis=-1):
    return jax.nn.softmax(x, axis=axis)

def _gelu(x):
    return jax.nn.gelu(x, approximate=True)

def _silu(x):
    return jax.nn.silu(x)

def _sigmoid(x):
    return jax.nn.sigmoid(x)

def _layernorm(x, axis=-1, eps=1e-05):
    m = jnp.mean(x, axis=axis, keepdims=True)
    v = jnp.var(x, axis=axis, keepdims=True)
    return (x - m) / jnp.sqrt(v + eps)

def _scatter_add(tgt, idx, src, axis=0):
    return tgt.at[idx].add(src)

def _segment_sum(src, seg, n):
    return jax.ops.segment_sum(src, seg, n)
kernel_name = 'mk_adj_preln_d1_adj_r2_8334d9'

def setup_inputs(seed: int=0):
    np.random.seed(seed)
    _w = jnp.asarray

    def _rec_inputs():
        import jax
        import jax.numpy as jnp
        _gk = jax.random.key(seed)
        x = -0.0005207 + 1.001 * jax.random.normal(jax.random.fold_in(_gk, 1), (16, 512, 128), jnp.float32)
        _a = jax.random.bernoulli(jax.random.fold_in(_gk, 2), 0.0078125, (16, 512, 512))
        _a = jnp.logical_or(_a, jnp.swapaxes(_a, -1, -2))
        _a = jnp.logical_or(_a, jnp.eye(512, dtype=bool))
        adj = _a.astype(jnp.int32)
        return (x, adj)
    x, adj = _rec_inputs()

    def _L0_gnn_setup():
        import jax, jax.numpy as jnp
        import numpy as np
        BS, N, D, R = (16, 256, 128, 2)
        key = jax.random.key(seed)
        ks = jax.random.split(key, 9)
        s = 1.0 / np.sqrt(D)
        return {'encoded_spans': jax.random.normal(ks[0], (BS, N, D), dtype=jnp.float32), 'w_rel1': jax.random.normal(ks[1], (R, D, D), dtype=jnp.float32) * s, 'w_root1': jax.random.normal(ks[2], (D, D), dtype=jnp.float32) * s, 'b1': jnp.zeros((D,), dtype=jnp.float32), 'w_rel2': jax.random.normal(ks[3], (R, D, D), dtype=jnp.float32) * s, 'w_root2': jax.random.normal(ks[4], (D, D), dtype=jnp.float32) * s, 'b2': jnp.zeros((D,), dtype=jnp.float32), 'aug_adj': jax.random.randint(ks[5], (BS, N, N), 0, 16, dtype=jnp.int64), 'punct_graph': jax.random.randint(ks[6], (BS, N, N), 0, 16, dtype=jnp.int64)}
    _L0_gnn_all = _L0_gnn_setup()
    _L0_gnn_in = {k: v for k, v in _L0_gnn_all.items() if k in ('w_rel1', 'w_root1', 'b1', 'w_rel2', 'w_root2', 'b2')}
    del _L0_gnn_all
    return {'x': x, 'adj': adj, 'L0_gnn_w_rel1': _L0_gnn_in['w_rel1'], 'L0_gnn_w_root1': _L0_gnn_in['w_root1'], 'L0_gnn_b1': _L0_gnn_in['b1'], 'L0_gnn_w_rel2': _L0_gnn_in['w_rel2'], 'L0_gnn_w_root2': _L0_gnn_in['w_root2'], 'L0_gnn_b2': _L0_gnn_in['b2']}

def reference(x, adj, L0_gnn_w_rel1, L0_gnn_w_root1, L0_gnn_b1, L0_gnn_w_rel2, L0_gnn_w_root2, L0_gnn_b2):
    import jax
    import jax.numpy as jnp

    def _L0_gnn_ref(encoded_spans, w_rel1, w_root1, b1, w_rel2, w_root2, b2, aug_adj, punct_graph):
        import jax, jax.numpy as jnp
        import numpy as np
        BS, N, D, R = (16, 256, 128, 2)
        mask_punct = (punct_graph == 1) & (aug_adj != 1)
        mask_aug = aug_adj == 1
        masks = jnp.stack([mask_punct, mask_aug]).astype(encoded_spans.dtype)
        deg = jnp.maximum(masks.sum(axis=2), 1.0)[..., None]

        def conv(x, w_rel, w_root, b):
            out = jnp.einsum('bnd,de->bne', x, w_root) + b
            for r in range(R):
                agg = jnp.einsum('bij,bid->bjd', masks[r], x) / deg[r]
                out = out + jnp.einsum('bjd,de->bje', agg, w_rel[r])
            return out
        h = jax.nn.elu(conv(encoded_spans, w_rel1, w_root1, b1))
        h = jax.nn.elu(conv(h, w_rel2, w_root2, b2))
        return h
    h = jnp.maximum(_layernorm(x, axis=-1), 0.0)
    x = x + _L0_gnn_ref(h, L0_gnn_w_rel1, L0_gnn_w_root1, L0_gnn_b1, L0_gnn_w_rel2, L0_gnn_w_root2, L0_gnn_b2, adj, adj)
    return x

_drawn_inputs = setup_inputs


def setup_inputs(seed=0):
    import zlib

    import numpy as np

    out = dict(_drawn_inputs(seed))
    spreads = {'L0_gnn_b1': (0.0, 0.1), 'L0_gnn_b2': (0.0, 0.1)}
    factors = {}
    for name, (base, spread) in spreads.items():
        noise = np.random.default_rng([zlib.crc32(name.encode()), seed]).standard_normal(out[name].shape)
        drawn = base * np.exp(spread * noise) if base else spread * noise
        out[name] = jnp.asarray(drawn.astype(out[name].dtype))
    for name, factor in factors.items():
        out[name] = (out[name] * factor).astype(out[name].dtype)
    return out
```

```python
from contextlib import ExitStack

import concourse.bass as bass
from concourse import mybir

F32 = mybir.dt.float32
F32R = mybir.dt.float32r
BF16 = mybir.dt.bfloat16
I32 = mybir.dt.int32
ALU = mybir.AluOpType
ACT = mybir.ActivationFunctionType

P = 128
EPS = 1e-5
UNROLL = 2


class Batch:

    def __init__(self, step0, pairs, offset):
        self.value = step0 + offset
        self.parity = offset % 2
        self.earlier = pairs + offset // 2


def graph_block_kernel(nc, x, adj, w_rel1, w_root1, b1, w_rel2, w_root2, b2, out):
    BATCHES, N, D = x.shape
    K = N // P
    HALF = K // 2
    FIRST, LAST = -2, BATCHES + 1
    assert D == P and N == K * P and K % 2 == 0 and BATCHES % 2 == 0
    LOOP_FIRST = 2
    PAIRS = (BATCHES - 2 - LOOP_FIRST) // UNROLL

    x_rows = x.rearrange("b (k p) d -> b p k d", p=P)
    adj_rows = adj.rearrange("b (k p) j -> b p k j", p=P)
    out_rows = out.rearrange("b (k p) d -> b p k d", p=P)

    with ExitStack() as ctx:
        def sb(name, shape, dt):
            return ctx.enter_context(nc.sbuf_tensor(name, shape, dt))

        def psum(name, shape, dt):
            return ctx.enter_context(nc.psum_tensor(name, shape, dt))

        def sem(name):
            return ctx.enter_context(nc.semaphore(name))

        x_all = sb("x_all", [P, BATCHES * K, D], F32)
        adj_in = [sb(f"adj_in{i}", [P, K, N], I32) for i in range(2)]
        mask = [sb(f"mask{i}", [P, K, N], F32R) for i in range(2)]
        w_root = [sb(f"w_root_l{i}", [P, D], F32) for i in range(2)]
        w_rel = [sb(f"w_rel_l{i}", [P, D], F32) for i in range(2)]
        w_rel_empty = [sb(f"w_rel_empty_l{i}", [P, D], F32) for i in range(2)]
        bias_in = sb("bias_in", [P, 2], F32)
        bias = sb("bias", [P, 2], F32)
        zeros = sb("zeros", [P, 1], F32)
        ones = sb("ones", [P, 1], BF16)
        ident = sb("ident", [P, P], F32)
        minus_half = sb("minus_half", [P, K], F32)
        minus_one = sb("minus_one", [P, K], F32)
        eps = sb("eps", [P, K], F32)

        block_stats = sb("block_stats", [P, K, 6], F32)
        mean_var = sb("mean_var", [P, K, 2], F32)
        var_eps = sb("var_eps", [P, K], F32)
        neg_mean = sb("neg_mean", [P, K], F32)
        rstd = sb("rstd", [P, K], F32)
        shift = sb("shift", [P, K], F32)
        h0 = sb("h0", [P, K, D], F32)
        h0_hi = sb("h0_hi", [P, K, D], F32R)
        h0_lo = sb("h0_lo", [P, K, D], F32R)
        h0T = sb("h0T", [P, N], F32)
        h1_hi = sb("h1_hi", [P, K, D], F32R)
        h1_lo = sb("h1_lo", [P, K, D], F32R)
        h1T = [sb(f"h1T{i}", [P, N], F32) for i in range(2)]
        h2T = sb("h2T", [P, N], F32)
        expT = [sb(f"expT_l{i}", [P, N], F32) for i in range(2)]
        nT = [sb(f"nT_l{i}", [P, N], F32) for i in range(2)]
        deg = sb("deg", [P, K], F32)
        rdeg = sb("rdeg", [P, K], F32)
        rdeg_row = [sb(f"rdeg_row{i}", [P, N], F32) for i in range(2)]
        out_sb = [sb(f"out_sb{i}", [P, K, D], F32) for i in range(2)]

        agg_ps = [psum(f"agg_ps_l{i}", [P, N], F32) for i in range(2)]
        v_ps = [psum(f"v_ps_l{i}", [P, N], F32) for i in range(2)]
        h0T_ps = psum("h0T_ps", [P, N], F32)
        h1_ps = psum("h1_ps", [P, K, D], F32)
        h2_ps = psum("h2_ps", [P, K, D], F32)
        deg_ps = psum("deg_ps", [P, N], F32)

        x_loaded = [sem(f"x_loaded{i}") for i in range(2)]
        adj_loaded = [sem(f"adj_loaded{i}") for i in range(2)]
        out_stored = [sem(f"out_stored{i}") for i in range(2)]
        weights_loaded = sem("weights_loaded")
        constants_set = sem("constants_set")
        rstd_prep = sem("rstd_prep")
        rstd_done = sem("rstd_done")
        h0_lo_done = sem("h0_lo_done")
        h0_done = sem("h0_done")
        h0_hi_done = sem("h0_hi_done")
        h0T_done = sem("h0T_done")
        h1_hi_done = sem("h1_hi_done")
        rdeg_row_done = sem("rdeg_row_done")
        exp_done = [sem(f"exp_done_l{i}") for i in range(2)]
        mask_done = sem("mask_done")
        block_stats_done = sem("block_stats_done")
        stats_done = sem("stats_done")
        deg_done = sem("deg_done")
        rdeg_done = sem("rdeg_done")
        n_done = [sem(f"n_done_l{i}") for i in range(2)]
        expm1_done = [sem(f"expm1_done_l{i}") for i in range(2)]
        h_done = [sem(f"h_done_l{i}") for i in range(2)]
        h1_lo_done = sem("h1_lo_done")
        bias_done = sem("bias_done")
        out_done = sem("out_done")
        empty_relation_done = sem("empty_relation_done")
        agg_done = [sem(f"agg_done_l{i}") for i in range(2)]
        mask_half_used = sem("mask_half_used")
        linear_done = [sem(f"linear_done_l{i}") for i in range(2)]
        deg_summed = sem("deg_summed")
        h0_transposed = sem("h0_transposed")
        h1_transposed = sem("h1_transposed")
        h2_transposed = sem("h2_transposed")
        rdeg_spread = sem("rdeg_spread")

        def exists(batch):
            return not isinstance(batch.value, int) or 0 <= batch.value < BATCHES

        def wait(eng, semaphore, count):
            if not isinstance(count, int) or count > 0:
                eng.wait_ge(semaphore, count)

        def run_steps(eng, step):
            def peeled(s):
                step(lambda k: Batch(s - s % 2, (s - s % 2) // 2, s % 2 + k))

            for s in range(FIRST, LOOP_FIRST):
                peeled(s)
            with eng.Fori(0, PAIRS) as pair:
                for u in range(UNROLL):
                    step(lambda k, u=u: Batch(2 * pair, pair, LOOP_FIRST + u + k))
            for s in range(LOOP_FIRST + UNROLL * PAIRS, LAST + 1):
                peeled(s)

        def x_block(b, k):
            return x_all[:, bass.ds(b.value * K + k, 1), :]

        block = ctx.enter_context(nc.Block())

        @block.sync
        def _(sp):
            def load_x(b):
                wait(sp, stats_done, b.value - 1)
                sp.dma_start(x_all[:, bass.ds(b.value * K, K), :], x_rows[bass.ds(b.value, 1), :, :, :].rearrange("b p k d -> p (b k) d")
                             ).then_inc(x_loaded[b.parity], 16)

            def load_adj(b):
                wait(sp, mask_done, b.value - 1)
                sp.dma_start(adj_in[b.parity][:], adj_rows[bass.ds(b.value, 1), :, :, :].rearrange("b p k j -> p (b k) j")
                             ).then_inc(adj_loaded[b.parity], 16)

            def store(b):
                wait(sp, out_done, b.value + 1)
                sp.dma_start(out_rows[bass.ds(b.value, 1), :, :, :].rearrange("b p k d -> p (b k) d"), out_sb[b.parity][:]
                             ).then_inc(out_stored[b.parity], 16)

            def step(at):
                if exists(at(2)):
                    load_x(at(2))
                    load_adj(at(2))
                if exists(at(-2)):
                    store(at(-2))

            run_steps(sp, step)
            for stored in out_stored:
                sp.wait_ge(stored, 16 * BATCHES // 2)

        @block.tensor
        def _(pe):
            def bias_with_empty_relation():
                pe.wait_ge(constants_set, 1)
                pe.wait_ge(weights_loaded, 16 * 8)
                for layer in range(2):
                    mm = nc.tensor.matmul(deg_ps[:, layer:layer + 1], w_rel_empty[layer][:], zeros[:],
                                          start=True, stop=True)
                mm.then_inc(empty_relation_done, 1)

            def aggregate(layer, b, h_hi, h_lo):
                wait(pe, n_done[layer], b.value)
                for k in range(K):
                    nc.tensor.matmul(agg_ps[layer][:], h_hi[:, k, :], mask[b.parity][:, k, :],
                                     start=(k == 0), stop=False)
                    mm = nc.tensor.matmul(agg_ps[layer][:], h_lo[:, k, :], mask[b.parity][:, k, :],
                                          start=False, stop=(k == K - 1))
                    if layer == 1 and k == HALF - 1:
                        mm.then_inc(mask_half_used, 1)
                mm.then_inc(agg_done[layer], 1)

            def linear(layer, b, hT):
                wait(pe, h_done[layer], b.value)
                nc.tensor.matmul(v_ps[layer][:], w_root[layer][:], hT[:], start=True, stop=False)
                pe.wait_ge(n_done[layer], b.value + 1)
                nc.tensor.matmul(v_ps[layer][:], w_rel[layer][:], nT[layer][:], start=False, stop=True
                                 ).then_inc(linear_done[layer], 1)

            def layer1(b):
                pe.wait_ge(h0_hi_done, b.value + 1)
                pe.wait_ge(h0_lo_done, b.value + 1)
                aggregate(0, b, h0_hi, h0_lo)

            def layer2(b):
                pe.wait_ge(h1_hi_done, b.value + 1)
                pe.wait_ge(h1_lo_done, b.value + 1)
                aggregate(1, b, h1_hi, h1_lo)

            def sum_degrees(b):
                pe.wait_ge(mask_done, b.value + 1)
                pe.wait_ge(bias_done, 1)
                wait(pe, rdeg_row_done, b.value)
                halves = mask[b.parity][:].bitcast(BF16).rearrange("p k (j t) -> p k j t", t=2)
                for j in range(K):
                    for k in range(K):
                        mm = nc.tensor.matmul(deg_ps[:, j:j + 1], halves[:, k, j * P:(j + 1) * P, 1], ones[:],
                                              start=(k == 0), stop=(k == K - 1))
                mm.then_inc(deg_summed, 1)

            def spread_rdeg(b):
                pe.wait_ge(rdeg_done, b.value + 1)
                for j in range(K):
                    mm = nc.tensor.transpose(deg_ps[:, j * P:(j + 1) * P],
                                             rdeg[:, j:j + 1].to_broadcast([P, P]), ident[:])
                mm.then_inc(rdeg_spread, 1)

            def transpose_h0(b):
                pe.wait_ge(h0_done, b.value + 1)
                wait(pe, h0T_done, b.value)
                for k in range(K):
                    mm = nc.tensor.transpose(h0T_ps[:, k * P:(k + 1) * P], h0[:, k, :], ident[:])
                mm.then_inc(h0_transposed, 1)

            def transpose_h1(b):
                pe.wait_ge(h_done[0], b.value + 1)
                wait(pe, h1_lo_done, b.value)
                for k in range(K):
                    mm = nc.tensor.transpose(h1_ps[:, k, :], h1T[b.parity][:, k * P:(k + 1) * P], ident[:])
                mm.then_inc(h1_transposed, 1)

            def transpose_h2(b):
                pe.wait_ge(h_done[1], b.value + 1)
                wait(pe, out_done, b.value)
                for k in range(K):
                    mm = nc.tensor.transpose(h2_ps[:, k, :], h2T[:, k * P:(k + 1) * P], ident[:])
                mm.then_inc(h2_transposed, 1)

            def step(at):
                if exists(at(0)):
                    layer1(at(0))
                if exists(at(-2)):
                    transpose_h2(at(-2))
                if exists(at(-1)):
                    layer2(at(-1))
                if exists(at(0)):
                    pe.wait_ge(h0T_done, at(0).value + 1)
                    linear(0, at(0), h0T)
                if exists(at(-1)):
                    linear(1, at(-1), h1T[at(-1).parity])
                if exists(at(1)):
                    sum_degrees(at(1))
                    transpose_h0(at(1))
                if exists(at(0)):
                    transpose_h1(at(0))
                if exists(at(1)):
                    spread_rdeg(at(1))

            bias_with_empty_relation()
            run_steps(pe, step)

        @block.scalar
        def _(act):
            for layer, (rel, root, b) in enumerate(((w_rel1, w_root1, b1), (w_rel2, w_root2, b2))):
                act.dma_start(w_rel_empty[layer][:], rel[0]).then_inc(weights_loaded, 16)
                act.dma_start(w_rel[layer][:], rel[1]).then_inc(weights_loaded, 16)
                act.dma_start(w_root[layer][:], root).then_inc(weights_loaded, 16)
                act.dma_start(bias_in[:, layer:layer + 1], b.rearrange("(p a) -> p a", a=1)
                              ).then_inc(weights_loaded, 16)

            def round_h1(b):
                act.wait_ge(h1_transposed, b.value + 1)
                wait(act, agg_done[1], b.value)
                nc.scalar.activation(h1_hi[:], h1_ps[:], ACT.Copy).then_inc(h1_hi_done, 1)

            def copy_rdeg(b):
                act.wait_ge(rdeg_spread, b.value + 1)
                wait(act, n_done[1], b.value - 1)
                nc.scalar.activation(rdeg_row[b.parity][:], deg_ps[:], ACT.Copy).then_inc(rdeg_row_done, 1)

            def normalise(b):
                act.wait_ge(rstd_done, b.value + 1)
                wait(act, h0_transposed, b.value)
                wait(act, h0_lo_done, b.value)
                for k in range(K):
                    a = nc.scalar.activation(h0[:, k:k + 1, :], x_block(b, k), ACT.Relu,
                                             bias=shift[:, k:k + 1], scale=rstd[:, k:k + 1])
                a.then_inc(h0_done, 1)
                act.wait_ge(h0_done, b.value + 1)
                wait(act, agg_done[0], b.value)
                nc.scalar.activation(h0_hi[:], h0[:], ACT.Copy).then_inc(h0_hi_done, 1)

            def copy_h0T(b):
                act.wait_ge(h0_transposed, b.value + 1)
                wait(act, linear_done[0], b.value)
                nc.scalar.activation(h0T[:], h0T_ps[:], ACT.Copy).then_inc(h0T_done, 1)

            def exp(layer, b):
                act.wait_ge(linear_done[layer], b.value + 1)
                wait(act, h_done[layer], b.value)
                nc.scalar.activation(expT[layer][:], v_ps[layer][:], ACT.Exp, bias=bias[:, layer:layer + 1]
                                     ).then_inc(exp_done[layer], 1)

            def step(at):
                if exists(at(-1)):
                    round_h1(at(-1))
                if exists(at(0)):
                    copy_rdeg(at(0))
                if exists(at(1)):
                    normalise(at(1))
                if exists(at(0)):
                    exp(0, at(0))
                if exists(at(-1)):
                    exp(1, at(-1))
                if exists(at(1)):
                    copy_h0T(at(1))

            act.wait_ge(bias_done, 1)
            run_steps(act, step)

        @block.vector
        def _(dve):
            def add_bias():
                dve.wait_ge(empty_relation_done, 1)
                dve.wait_ge(weights_loaded, 16 * 8)
                nc.vector.tensor_tensor(bias[:], deg_ps[:, 0:2], bias_in[:], ALU.add).then_inc(bias_done, 1)

            def rest_h1(b):
                dve.wait_ge(h1_hi_done, b.value + 1)
                wait(dve, agg_done[1], b.value)
                nc.vector.tensor_tensor(h1_lo[:], h1_ps[:], h1_hi[:].bitcast(F32), ALU.subtract
                                        ).then_inc(h1_lo_done, 1)

            def divide_by_degree(layer, b):
                dve.wait_ge(agg_done[layer], b.value + 1)
                dve.wait_ge(rdeg_row_done, b.value + 1)
                wait(dve, linear_done[layer], b.value)
                nc.vector.tensor_tensor(nT[layer][:], agg_ps[layer][:], rdeg_row[b.parity][:], ALU.mult
                                        ).then_inc(n_done[layer], 1)

            def make_mask(b, half):
                ks = slice(half * HALF, (half + 1) * HALF)
                if half == 0:
                    dve.wait_ge(adj_loaded[b.parity], 16 * (b.earlier + 1))
                    wait(dve, mask_half_used, b.value - 1)
                else:
                    wait(dve, agg_done[1], b.value - 1)
                ts = nc.vector.tensor_scalar(mask[b.parity][:, ks, :], adj_in[b.parity][:, ks, :],
                                             1.0, None, ALU.is_equal)
                if half == 1:
                    ts.then_inc(mask_done, 1)

            def statistics(b):
                dve.wait_ge(x_loaded[b.parity], 16 * (b.earlier + 1))
                wait(dve, stats_done, b.value)
                for k in range(K):
                    bn = nc.vector.bn_stats(block_stats[:, k, :], x_block(b, k))
                bn.then_inc(block_stats_done, 1)

            def await_statistics(b):
                dve.wait_ge(block_stats_done, b.value + 1)
                wait(dve, rstd_done, b.value)

            def mean_and_variance(b):
                for k in range(K):
                    bn = nc.vector.bn_aggr(mean_var[:, k, :], block_stats[:, k, :])
                bn.then_inc(stats_done, 1)

            def expm1(layer, b):
                dve.wait_ge(exp_done[layer], b.value + 1)
                nc.vector.tensor_scalar(expT[layer][:], expT[layer][:], -1.0, 0.0, ALU.add, ALU.min
                                        ).then_inc(expm1_done[layer], 1)

            def elu(layer, b, hT):
                dve.wait_ge(expm1_done[layer], b.value + 1)
                if layer == 0:
                    wait(dve, linear_done[1], b.value - 1)
                else:
                    wait(dve, h2_transposed, b.value)
                nc.vector.scalar_tensor_tensor(hT[:], v_ps[layer][:], bias[:, layer:layer + 1],
                                               expT[layer][:], ALU.add, ALU.max).then_inc(h_done[layer], 1)

            def reciprocal_degree(b):
                dve.wait_ge(deg_summed, b.value + 1)
                nc.vector.tensor_scalar(deg[:], deg_ps[:, 0:K], 1.0, None, ALU.max).then_inc(deg_done, 1)
                dve.wait_ge(deg_done, b.value + 1)
                wait(dve, rdeg_spread, b.value)
                nc.vector.reciprocal(rdeg[:], deg[:]).then_inc(rdeg_done, 1)

            def add_x(b):
                dve.wait_ge(h2_transposed, b.value + 1)
                wait(dve, out_stored[b.parity], 16 * b.earlier)
                nc.vector.tensor_tensor(out_sb[b.parity][:], h2_ps[:], x_all[:, bass.ds(b.value * K, K), :],
                                        ALU.add).then_inc(out_done, 1)

            def step(at):
                if exists(at(-1)):
                    rest_h1(at(-1))
                if exists(at(0)):
                    divide_by_degree(0, at(0))
                if exists(at(-2)):
                    add_x(at(-2))
                if exists(at(1)):
                    make_mask(at(1), 0)
                if exists(at(2)):
                    statistics(at(2))
                if exists(at(-1)):
                    divide_by_degree(1, at(-1))
                if exists(at(2)):
                    await_statistics(at(2))
                if exists(at(1)):
                    make_mask(at(1), 1)
                if exists(at(2)):
                    mean_and_variance(at(2))
                if exists(at(0)):
                    expm1(0, at(0))
                    elu(0, at(0), h1T[at(0).parity])
                if exists(at(1)):
                    reciprocal_degree(at(1))
                if exists(at(-1)):
                    expm1(1, at(-1))
                    elu(1, at(-1), h2T)

            add_bias()
            run_steps(dve, step)

        @block.gpsimd
        def _(pool):
            nc.gpsimd.memset(ones[:], 1.0)
            nc.gpsimd.memset(minus_half[:], -0.5)
            nc.gpsimd.memset(minus_one[:], -1.0)
            nc.gpsimd.memset(eps[:], EPS)
            nc.gpsimd.memset(zeros[:], 0.0)
            nc.gpsimd.memset(ident[:], 0.0).then_inc(rstd_prep, 1)
            pool.wait_ge(rstd_prep, 1)
            nc.gpsimd.affine_select(out=ident[:], in_=ident[:], compare_op=ALU.not_equal, fill=1.0, base=0,
                                    pattern=[[-1, P]], channel_multiplier=1).then_inc(constants_set, 1)

            def inverse_deviation(b):
                pool.wait_ge(stats_done, b.value + 1)
                wait(pool, h0_done, b.value)
                nc.gpsimd.tensor_tensor(var_eps[:], mean_var[:, :, 1], eps[:], ALU.add)
                nc.gpsimd.tensor_tensor(neg_mean[:], mean_var[:, :, 0], minus_one[:], ALU.mult
                                        ).then_inc(rstd_prep, 1)
                pool.wait_ge(rstd_prep, 2 * b.value + 2)
                nc.gpsimd.tensor_tensor(rstd[:], var_eps[:], minus_half[:], ALU.pow).then_inc(rstd_prep, 1)
                pool.wait_ge(rstd_prep, 2 * b.value + 3)
                nc.gpsimd.tensor_tensor(shift[:], neg_mean[:], rstd[:], ALU.mult).then_inc(rstd_done, 1)

            def rest_h0(b):
                pool.wait_ge(h0_hi_done, b.value + 1)
                wait(pool, agg_done[0], b.value)
                nc.gpsimd.tensor_tensor(h0_lo[:], h0[:], h0_hi[:].bitcast(F32), ALU.subtract
                                        ).then_inc(h0_lo_done, 1)

            def step(at):
                if exists(at(1)):
                    rest_h0(at(1))
                if exists(at(2)):
                    inverse_deviation(at(2))

            run_steps(pool, step)


_INS = ['x', 'adj', 'L0_gnn_w_rel1', 'L0_gnn_w_root1', 'L0_gnn_b1', 'L0_gnn_w_rel2', 'L0_gnn_w_root2', 'L0_gnn_b2']


def kernel(**inputs):
    import numpy as _np
    import concourse.bacc as _bacc
    from concourse import mybir as _mybir
    from concourse.bass_utils import run_bass_kernel_spmd as _run

    nc = _bacc.Bacc("TRN2", target_bir_lowering=False, num_devices=1)
    arrays, args = {}, []
    for name in _INS:
        a = _np.ascontiguousarray(inputs[name])
        arrays[f"in_{name}_dram"] = a
        args.append(nc.dram_tensor(f"in_{name}_dram", a.shape, _mybir.dt.from_np(a.dtype), kind="ExternalInput").ap())
    out = nc.dram_tensor("out_dram", inputs["x"].shape, _mybir.dt.float32, kind="ExternalOutput").ap()
    graph_block_kernel(nc, *args, out)
    r = _run(nc, [arrays], core_ids=[0])
    return r.results[0]["out_dram"]
```

```python
from contextlib import ExitStack

import concourse.bass as bass
from concourse import mybir

F32 = mybir.dt.float32
F32R = mybir.dt.float32r
BF16 = mybir.dt.bfloat16
I32 = mybir.dt.int32
ALU = mybir.AluOpType
ACT = mybir.ActivationFunctionType

P = 128
EPS = 1e-5
UNROLL = 2


class Batch:

    def __init__(self, step0, pairs, offset):
        self.value = step0 + offset
        self.parity = offset % 2
        self.earlier = pairs + offset // 2


def graph_block_kernel(nc, x, adj, w_rel1, w_root1, b1, w_rel2, w_root2, b2, out):
    BATCHES, N, D = x.shape
    K = N // P
    HALF = K // 2
    FIRST, LAST = -2, BATCHES + 1
    assert D == P and N == K * P and K % 2 == 0 and BATCHES % 2 == 0
    LOOP_FIRST = 2
    PAIRS = (BATCHES - 2 - LOOP_FIRST) // UNROLL

    x_rows = x.rearrange("b (k p) d -> b p k d", p=P)
    adj_rows = adj.rearrange("b (k p) j -> b p k j", p=P)
    out_rows = out.rearrange("b (k p) d -> b p k d", p=P)

    with ExitStack() as ctx:
        def sb(name, shape, dt):
            return ctx.enter_context(nc.sbuf_tensor(name, shape, dt))

        def psum(name, shape, dt):
            return ctx.enter_context(nc.psum_tensor(name, shape, dt))

        def sem(name):
            return ctx.enter_context(nc.semaphore(name))

        x_all = sb("x_all", [P, BATCHES * K, D], F32)
        adj_in = [sb(f"adj_in{i}", [P, K, N], I32) for i in range(2)]
        mask = [sb(f"mask{i}", [P, K, N], F32R) for i in range(2)]
        ROOT, REL = 0, 1
        weights = sb("weights", [P, 2, 2, D], F32)
        weights_hi = sb("weights_hi", [P, 2, 2, D], F32R)
        weights_lo = sb("weights_lo", [P, 2, 2, D], F32R)
        w_rel_empty = [sb(f"w_rel_empty_l{i}", [P, D], F32) for i in range(2)]
        bias_in = sb("bias_in", [P, 2], F32)
        bias = sb("bias", [P, 2], F32)
        zeros = sb("zeros", [P, 1], F32)
        ones = sb("ones", [P, 1], BF16)
        ident = sb("ident", [P, P], F32)
        minus_half = sb("minus_half", [P, K], F32)
        minus_one = sb("minus_one", [P, K], F32)
        eps = sb("eps", [P, K], F32)

        block_stats = sb("block_stats", [P, K, 6], F32)
        mean_var = sb("mean_var", [P, K, 2], F32)
        var_eps = sb("var_eps", [P, K], F32)
        neg_mean = sb("neg_mean", [P, K], F32)
        rstd = sb("rstd", [P, K], F32)
        shift = sb("shift", [P, K], F32)
        h0 = sb("h0", [P, K, D], F32)
        h0_hi = sb("h0_hi", [P, K, D], F32R)
        h0_lo = sb("h0_lo", [P, K, D], F32R)
        h0T_hi = sb("h0T_hi", [P, N], F32R)
        h0T_lo = sb("h0T_lo", [P, N], F32R)
        h1_hi = sb("h1_hi", [P, K, D], F32R)
        h1_lo = sb("h1_lo", [P, K, D], F32R)
        h1T = sb("h1T", [P, N], F32)
        h1T_hi = sb("h1T_hi", [P, N], F32R)
        h1T_lo = sb("h1T_lo", [P, N], F32R)
        h2T = sb("h2T", [P, N], F32)
        expT = [sb(f"expT_l{i}", [P, N], F32) for i in range(2)]
        nT = [sb(f"nT_l{i}", [P, N], F32) for i in range(2)]
        nT_hi = [sb(f"nT_hi_l{i}", [P, N], F32R) for i in range(2)]
        nT_lo = [sb(f"nT_lo_l{i}", [P, N], F32R) for i in range(2)]
        deg = sb("deg", [P, K], F32)
        rdeg = sb("rdeg", [P, K], F32)
        rdeg_row = [sb(f"rdeg_row{i}", [P, N], F32) for i in range(2)]
        out_sb = [sb(f"out_sb{i}", [P, K, D], F32) for i in range(2)]

        agg_ps = [psum(f"agg_ps_l{i}", [P, N], F32) for i in range(2)]
        v_ps = [psum(f"v_ps_l{i}", [P, N], F32) for i in range(2)]
        h0T_ps = psum("h0T_ps", [P, N], F32)
        h1_ps = psum("h1_ps", [P, K, D], F32)
        h2_ps = psum("h2_ps", [P, K, D], F32)
        deg_ps = psum("deg_ps", [P, N], F32)

        x_loaded = [sem(f"x_loaded{i}") for i in range(2)]
        adj_loaded = [sem(f"adj_loaded{i}") for i in range(2)]
        out_stored = [sem(f"out_stored{i}") for i in range(2)]
        weights_loaded = sem("weights_loaded")
        constants_set = sem("constants_set")
        rstd_prep = sem("rstd_prep")
        rstd_done = sem("rstd_done")
        h0_lo_done = sem("h0_lo_done")
        h1T_lo_done = sem("h1T_lo_done")
        n_lo_done = [sem(f"n_lo_done_l{i}") for i in range(2)]
        weights_lo_done = sem("weights_lo_done")
        h0_done = sem("h0_done")
        h0_hi_done = sem("h0_hi_done")
        h0T_hi_done = sem("h0T_hi_done")
        h1T_hi_done = sem("h1T_hi_done")
        n_hi_done = [sem(f"n_hi_done_l{i}") for i in range(2)]
        weights_hi_done = sem("weights_hi_done")
        h1_hi_done = sem("h1_hi_done")
        rdeg_row_done = sem("rdeg_row_done")
        exp_done = [sem(f"exp_done_l{i}") for i in range(2)]
        mask_done = sem("mask_done")
        block_stats_done = sem("block_stats_done")
        stats_done = sem("stats_done")
        deg_done = sem("deg_done")
        rdeg_done = sem("rdeg_done")
        n_done = [sem(f"n_done_l{i}") for i in range(2)]
        expm1_done = [sem(f"expm1_done_l{i}") for i in range(2)]
        h_done = [sem(f"h_done_l{i}") for i in range(2)]
        h1_lo_done = sem("h1_lo_done")
        h0T_lo_done = sem("h0T_lo_done")
        bias_done = sem("bias_done")
        out_done = sem("out_done")
        empty_relation_done = sem("empty_relation_done")
        agg_done = [sem(f"agg_done_l{i}") for i in range(2)]
        mask_half_used = sem("mask_half_used")
        linear_done = [sem(f"linear_done_l{i}") for i in range(2)]
        deg_summed = sem("deg_summed")
        h0_transposed = sem("h0_transposed")
        h1_transposed = sem("h1_transposed")
        h2_transposed = sem("h2_transposed")
        rdeg_spread = sem("rdeg_spread")

        def exists(batch):
            return not isinstance(batch.value, int) or 0 <= batch.value < BATCHES

        def wait(eng, semaphore, count):
            if not isinstance(count, int) or count > 0:
                eng.wait_ge(semaphore, count)

        def run_steps(eng, step, before_step_0=None):
            def peeled(s):
                step(lambda k: Batch(s - s % 2, (s - s % 2) // 2, s % 2 + k))

            for s in range(FIRST, LOOP_FIRST):
                if s == 0 and before_step_0:
                    before_step_0()
                peeled(s)
            with eng.Fori(0, PAIRS) as pair:
                for u in range(UNROLL):
                    step(lambda k, u=u: Batch(2 * pair, pair, LOOP_FIRST + u + k))
            for s in range(LOOP_FIRST + UNROLL * PAIRS, LAST + 1):
                peeled(s)

        def x_block(b, k):
            return x_all[:, bass.ds(b.value * K + k, 1), :]

        block = ctx.enter_context(nc.Block())

        @block.sync
        def _(sp):
            def load_x(b):
                wait(sp, stats_done, b.value - 1)
                sp.dma_start(x_all[:, bass.ds(b.value * K, K), :], x_rows[bass.ds(b.value, 1), :, :, :].rearrange("b p k d -> p (b k) d")
                             ).then_inc(x_loaded[b.parity], 16)

            def load_adj(b):
                wait(sp, mask_done, b.value - 1)
                sp.dma_start(adj_in[b.parity][:], adj_rows[bass.ds(b.value, 1), :, :, :].rearrange("b p k j -> p (b k) j")
                             ).then_inc(adj_loaded[b.parity], 16)

            def store(b):
                wait(sp, out_done, b.value + 1)
                sp.dma_start(out_rows[bass.ds(b.value, 1), :, :, :].rearrange("b p k d -> p (b k) d"), out_sb[b.parity][:]
                             ).then_inc(out_stored[b.parity], 16)

            def step(at):
                if exists(at(2)):
                    load_x(at(2))
                    load_adj(at(2))
                if exists(at(-2)):
                    store(at(-2))

            run_steps(sp, step)
            for stored in out_stored:
                sp.wait_ge(stored, 16 * BATCHES // 2)

        @block.tensor
        def _(pe):
            def bias_with_empty_relation():
                pe.wait_ge(weights_lo_done, 1)
                for layer in range(2):
                    mm = nc.tensor.matmul(v_ps[1][:, layer:layer + 1], w_rel_empty[layer][:], zeros[:],
                                          start=True, stop=True)
                mm.then_inc(empty_relation_done, 1)

            def aggregate(layer, b, h_hi, h_hi_done, h_lo, h_lo_done):
                wait(pe, n_done[layer], b.value)
                pe.wait_ge(h_hi_done, b.value + 1)
                for k in range(K):
                    nc.tensor.matmul(agg_ps[layer][:], h_hi[:, k, :], mask[b.parity][:, k, :],
                                     start=(k == 0), stop=False)
                pe.wait_ge(h_lo_done, b.value + 1)
                for k in range(K):
                    mm = nc.tensor.matmul(agg_ps[layer][:], h_lo[:, k, :], mask[b.parity][:, k, :],
                                          start=False, stop=(k == K - 1))
                    if layer == 1 and k == HALF - 1:
                        mm.then_inc(mask_half_used, 1)
                mm.then_inc(agg_done[layer], 1)

            def product(layer, which, hT_hi, hT_lo, hT_lo_done, b):
                v = v_ps[layer][:]
                nc.tensor.matmul(v, weights_hi[:, layer, which, :], hT_hi[:], start=(which == ROOT), stop=False)
                nc.tensor.matmul(v, weights_lo[:, layer, which, :], hT_hi[:], start=False, stop=False)
                pe.wait_ge(hT_lo_done, b.value + 1)
                return nc.tensor.matmul(v, weights_hi[:, layer, which, :], hT_lo[:], start=False, stop=(which == REL))

            def root(layer, b, hT_hi, hT_hi_done, hT_lo, hT_lo_done):
                wait(pe, h_done[layer], b.value)
                pe.wait_ge(hT_hi_done, b.value + 1)
                product(layer, ROOT, hT_hi, hT_lo, hT_lo_done, b)

            def rel(layer, b):
                pe.wait_ge(n_hi_done[layer], b.value + 1)
                product(layer, REL, nT_hi[layer], nT_lo[layer], n_lo_done[layer], b).then_inc(linear_done[layer], 1)

            def sum_degrees(b):
                pe.wait_ge(mask_done, b.value + 1)
                pe.wait_ge(constants_set, 1)
                wait(pe, rdeg_row_done, b.value)
                halves = mask[b.parity][:].bitcast(BF16).rearrange("p k (j t) -> p k j t", t=2)
                for j in range(K):
                    for k in range(K):
                        mm = nc.tensor.matmul(deg_ps[:, j:j + 1], halves[:, k, j * P:(j + 1) * P, 1], ones[:],
                                              start=(k == 0), stop=(k == K - 1))
                mm.then_inc(deg_summed, 1)

            def spread_rdeg(b):
                pe.wait_ge(rdeg_done, b.value + 1)
                for j in range(K):
                    mm = nc.tensor.transpose(deg_ps[:, j * P:(j + 1) * P],
                                             rdeg[:, j:j + 1].to_broadcast([P, P]), ident[:])
                mm.then_inc(rdeg_spread, 1)

            def transpose_h0(b):
                pe.wait_ge(h0_done, b.value + 1)
                wait(pe, h0T_lo_done, b.value)
                for k in range(K):
                    mm = nc.tensor.transpose(h0T_ps[:, k * P:(k + 1) * P], h0[:, k, :], ident[:])
                mm.then_inc(h0_transposed, 1)

            def transpose_h1(b):
                pe.wait_ge(h_done[0], b.value + 1)
                wait(pe, h1_lo_done, b.value)
                for k in range(K):
                    mm = nc.tensor.transpose(h1_ps[:, k, :], h1T[:, k * P:(k + 1) * P], ident[:])
                mm.then_inc(h1_transposed, 1)

            def transpose_h2(b):
                pe.wait_ge(h_done[1], b.value + 1)
                wait(pe, out_done, b.value)
                for k in range(K):
                    mm = nc.tensor.transpose(h2_ps[:, k, :], h2T[:, k * P:(k + 1) * P], ident[:])
                mm.then_inc(h2_transposed, 1)

            def step(at):
                if exists(at(0)):
                    aggregate(0, at(0), h0_hi, h0_hi_done, h0_lo, h0_lo_done)
                if exists(at(-1)):
                    transpose_h1(at(-1))
                if exists(at(0)):
                    root(0, at(0), h0T_hi, h0T_hi_done, h0T_lo, h0T_lo_done)
                if exists(at(-2)):
                    transpose_h2(at(-2))
                if exists(at(-1)):
                    aggregate(1, at(-1), h1_hi, h1_hi_done, h1_lo, h1_lo_done)
                if exists(at(0)):
                    rel(0, at(0))
                if exists(at(-1)):
                    root(1, at(-1), h1T_hi, h1T_hi_done, h1T_lo, h1T_lo_done)
                if exists(at(1)):
                    transpose_h0(at(1))
                    sum_degrees(at(1))
                if exists(at(-1)):
                    rel(1, at(-1))
                if exists(at(1)):
                    spread_rdeg(at(1))

            run_steps(pe, step, bias_with_empty_relation)

        @block.scalar
        def _(act):
            for layer, (rel, root, b) in enumerate(((w_rel1, w_root1, b1), (w_rel2, w_root2, b2))):
                act.dma_start(w_rel_empty[layer][:], rel[0]).then_inc(weights_loaded, 16)
                act.dma_start(weights[:, layer, REL, :], rel[1]).then_inc(weights_loaded, 16)
                act.dma_start(weights[:, layer, ROOT, :], root).then_inc(weights_loaded, 16)
                act.dma_start(bias_in[:, layer:layer + 1], b.rearrange("(p a) -> p a", a=1)
                              ).then_inc(weights_loaded, 16)

            def round_h1(b):
                act.wait_ge(h1_transposed, b.value + 1)
                wait(act, agg_done[1], b.value)
                nc.scalar.activation(h1_hi[:], h1_ps[:], ACT.Copy).then_inc(h1_hi_done, 1)

            def copy_rdeg(b):
                act.wait_ge(rdeg_spread, b.value + 1)
                wait(act, n_done[1], b.value - 1)
                nc.scalar.activation(rdeg_row[b.parity][:], deg_ps[:], ACT.Copy).then_inc(rdeg_row_done, 1)

            def normalise(b):
                act.wait_ge(rstd_done, b.value + 1)
                wait(act, h0_transposed, b.value)
                wait(act, h0_lo_done, b.value)
                normalise_blocks(b, range(HALF))

            def normalise_blocks(b, blocks):
                for k in blocks:
                    a = nc.scalar.activation(h0[:, k:k + 1, :], x_block(b, k), ACT.Relu,
                                             bias=shift[:, k:k + 1], scale=rstd[:, k:k + 1])
                return a

            def normalise_and_round(b):
                normalise_blocks(b, range(HALF, K)).then_inc(h0_done, 1)
                act.wait_ge(h0_done, b.value + 1)
                wait(act, agg_done[0], b.value)
                nc.scalar.activation(h0_hi[:], h0[:], ACT.Copy).then_inc(h0_hi_done, 1)

            def round_h0T(b):
                act.wait_ge(h0_transposed, b.value + 1)
                wait(act, linear_done[0], b.value)
                nc.scalar.activation(h0T_hi[:], h0T_ps[:], ACT.Copy).then_inc(h0T_hi_done, 1)

            def round_h1T(b):
                act.wait_ge(h_done[0], b.value + 1)
                wait(act, linear_done[1], b.value)
                nc.scalar.activation(h1T_hi[:], h1T[:], ACT.Copy).then_inc(h1T_hi_done, 1)

            def round_n(layer, b):
                act.wait_ge(n_done[layer], b.value + 1)
                wait(act, linear_done[layer], b.value)
                nc.scalar.activation(nT_hi[layer][:], nT[layer][:], ACT.Copy).then_inc(n_hi_done[layer], 1)

            def exp(layer, b):
                act.wait_ge(bias_done, 1)
                act.wait_ge(linear_done[layer], b.value + 1)
                wait(act, h_done[layer], b.value)
                nc.scalar.activation(expT[layer][:], v_ps[layer][:], ACT.Exp, bias=bias[:, layer:layer + 1]
                                     ).then_inc(exp_done[layer], 1)

            def step(at):
                if exists(at(-2)):
                    exp(1, at(-2))
                if exists(at(0)):
                    copy_rdeg(at(0))
                if exists(at(-1)):
                    round_h1T(at(-1))
                if exists(at(1)):
                    normalise(at(1))
                if exists(at(-1)):
                    round_h1(at(-1))
                if exists(at(0)):
                    round_n(0, at(0))
                if exists(at(1)):
                    normalise_and_round(at(1))
                if exists(at(-1)):
                    round_n(1, at(-1))
                if exists(at(0)):
                    exp(0, at(0))
                if exists(at(1)):
                    round_h0T(at(1))

            def round_weights():
                act.wait_ge(weights_loaded, 16 * 8)
                nc.scalar.activation(weights_hi[:], weights[:], ACT.Copy).then_inc(weights_hi_done, 1)

            run_steps(act, step, round_weights)

        @block.vector
        def _(dve):
            def add_bias():
                dve.wait_ge(empty_relation_done, 1)
                dve.wait_ge(weights_loaded, 16 * 8)
                nc.vector.tensor_tensor(bias[:], v_ps[1][:, 0:2], bias_in[:], ALU.add).then_inc(bias_done, 1)

            def rest_h1(b):
                dve.wait_ge(h1_hi_done, b.value + 1)
                wait(dve, agg_done[1], b.value)
                nc.vector.tensor_tensor(h1_lo[:], h1_ps[:], h1_hi[:].bitcast(F32), ALU.subtract
                                        ).then_inc(h1_lo_done, 1)

            def divide_by_degree(layer, b):
                dve.wait_ge(agg_done[layer], b.value + 1)
                dve.wait_ge(rdeg_row_done, b.value + 1)
                wait(dve, n_lo_done[layer], b.value)
                nc.vector.tensor_tensor(nT[layer][:], agg_ps[layer][:], rdeg_row[b.parity][:], ALU.mult
                                        ).then_inc(n_done[layer], 1)

            def rest_h0T(b):
                dve.wait_ge(h0T_hi_done, b.value + 1)
                wait(dve, linear_done[0], b.value)
                nc.vector.tensor_tensor(h0T_lo[:], h0T_ps[:], h0T_hi[:].bitcast(F32), ALU.subtract
                                        ).then_inc(h0T_lo_done, 1)

            def make_mask(b, half):
                ks = slice(half * HALF, (half + 1) * HALF)
                if half == 0:
                    dve.wait_ge(adj_loaded[b.parity], 16 * (b.earlier + 1))
                    wait(dve, mask_half_used, b.value - 1)
                else:
                    wait(dve, agg_done[1], b.value - 1)
                ts = nc.vector.tensor_scalar(mask[b.parity][:, ks, :], adj_in[b.parity][:, ks, :],
                                             1.0, None, ALU.is_equal)
                if half == 1:
                    ts.then_inc(mask_done, 1)

            def statistics(b):
                dve.wait_ge(x_loaded[b.parity], 16 * (b.earlier + 1))
                wait(dve, stats_done, b.value)
                for k in range(K):
                    bn = nc.vector.bn_stats(block_stats[:, k, :], x_block(b, k))
                bn.then_inc(block_stats_done, 1)

            def await_statistics(b):
                dve.wait_ge(block_stats_done, b.value + 1)
                wait(dve, rstd_done, b.value)

            def mean_and_variance(b):
                for k in range(K):
                    bn = nc.vector.bn_aggr(mean_var[:, k, :], block_stats[:, k, :])
                bn.then_inc(stats_done, 1)

            def expm1(layer, b):
                dve.wait_ge(exp_done[layer], b.value + 1)
                nc.vector.tensor_scalar(expT[layer][:], expT[layer][:], -1.0, 0.0, ALU.add, ALU.min
                                        ).then_inc(expm1_done[layer], 1)

            def elu(layer, b, hT):
                dve.wait_ge(expm1_done[layer], b.value + 1)
                if layer == 0:
                    wait(dve, h1_transposed, b.value)
                    wait(dve, h1T_lo_done, b.value)
                else:
                    wait(dve, h2_transposed, b.value)
                nc.vector.scalar_tensor_tensor(hT[:], v_ps[layer][:], bias[:, layer:layer + 1],
                                               expT[layer][:], ALU.add, ALU.max).then_inc(h_done[layer], 1)

            def reciprocal_degree(b):
                dve.wait_ge(deg_summed, b.value + 1)
                nc.vector.tensor_scalar(deg[:], deg_ps[:, 0:K], 1.0, None, ALU.max).then_inc(deg_done, 1)
                dve.wait_ge(deg_done, b.value + 1)
                wait(dve, rdeg_spread, b.value)
                nc.vector.reciprocal(rdeg[:], deg[:]).then_inc(rdeg_done, 1)

            def add_x(b):
                dve.wait_ge(h2_transposed, b.value + 1)
                wait(dve, out_stored[b.parity], 16 * b.earlier)
                nc.vector.tensor_tensor(out_sb[b.parity][:], h2_ps[:], x_all[:, bass.ds(b.value * K, K), :],
                                        ALU.add).then_inc(out_done, 1)

            def step(at):
                if exists(at(-2)):
                    expm1(1, at(-2))
                    elu(1, at(-2), h2T)
                if exists(at(0)):
                    divide_by_degree(0, at(0))
                if exists(at(-1)):
                    rest_h1(at(-1))
                if exists(at(-2)):
                    add_x(at(-2))
                if exists(at(2)):
                    statistics(at(2))
                if exists(at(-1)):
                    divide_by_degree(1, at(-1))
                if exists(at(1)):
                    make_mask(at(1), 0)
                if exists(at(2)):
                    await_statistics(at(2))
                if exists(at(1)):
                    make_mask(at(1), 1)
                if exists(at(0)):
                    expm1(0, at(0))
                if exists(at(2)):
                    mean_and_variance(at(2))
                if exists(at(1)):
                    reciprocal_degree(at(1))
                if exists(at(0)):
                    elu(0, at(0), h1T)
                if exists(at(1)):
                    rest_h0T(at(1))

            run_steps(dve, step, add_bias)

        @block.gpsimd
        def _(pool):
            nc.gpsimd.memset(ones[:], 1.0)
            nc.gpsimd.memset(minus_half[:], -0.5)
            nc.gpsimd.memset(minus_one[:], -1.0)
            nc.gpsimd.memset(eps[:], EPS)
            nc.gpsimd.memset(zeros[:], 0.0)
            nc.gpsimd.memset(ident[:], 0.0).then_inc(rstd_prep, 1)
            pool.wait_ge(rstd_prep, 1)
            nc.gpsimd.affine_select(out=ident[:], in_=ident[:], compare_op=ALU.not_equal, fill=1.0, base=0,
                                    pattern=[[-1, P]], channel_multiplier=1).then_inc(constants_set, 1)

            def inverse_deviation(b):
                pool.wait_ge(stats_done, b.value + 1)
                wait(pool, h0_done, b.value)
                nc.gpsimd.tensor_tensor(var_eps[:], mean_var[:, :, 1], eps[:], ALU.add)
                nc.gpsimd.tensor_tensor(neg_mean[:], mean_var[:, :, 0], minus_one[:], ALU.mult
                                        ).then_inc(rstd_prep, 1)
                pool.wait_ge(rstd_prep, 2 * b.value + 2)
                nc.gpsimd.tensor_tensor(rstd[:], var_eps[:], minus_half[:], ALU.pow).then_inc(rstd_prep, 1)
                pool.wait_ge(rstd_prep, 2 * b.value + 3)
                nc.gpsimd.tensor_tensor(shift[:], neg_mean[:], rstd[:], ALU.mult).then_inc(rstd_done, 1)

            def rest_h0(b):
                pool.wait_ge(h0_hi_done, b.value + 1)
                wait(pool, agg_done[0], b.value)
                nc.gpsimd.tensor_tensor(h0_lo[:], h0[:], h0_hi[:].bitcast(F32), ALU.subtract
                                        ).then_inc(h0_lo_done, 1)

            def rest_h1T(b):
                pool.wait_ge(h1T_hi_done, b.value + 1)
                wait(pool, linear_done[1], b.value)
                nc.gpsimd.tensor_tensor(h1T_lo[:], h1T[:], h1T_hi[:].bitcast(F32), ALU.subtract
                                        ).then_inc(h1T_lo_done, 1)

            def rest_n(layer, b):
                pool.wait_ge(n_hi_done[layer], b.value + 1)
                wait(pool, linear_done[layer], b.value)
                nc.gpsimd.tensor_tensor(nT_lo[layer][:], nT[layer][:], nT_hi[layer][:].bitcast(F32), ALU.subtract
                                        ).then_inc(n_lo_done[layer], 1)

            def step(at):
                if exists(at(-1)):
                    rest_h1T(at(-1))
                if exists(at(0)):
                    rest_n(0, at(0))
                if exists(at(1)):
                    rest_h0(at(1))
                if exists(at(-1)):
                    rest_n(1, at(-1))
                if exists(at(2)):
                    inverse_deviation(at(2))


            def rest_weights():
                pool.wait_ge(weights_hi_done, 1)
                nc.gpsimd.tensor_tensor(weights_lo[:], weights[:], weights_hi[:].bitcast(F32), ALU.subtract
                                        ).then_inc(weights_lo_done, 1)

            run_steps(pool, step, rest_weights)


_INS = ['x', 'adj', 'L0_gnn_w_rel1', 'L0_gnn_w_root1', 'L0_gnn_b1', 'L0_gnn_w_rel2', 'L0_gnn_w_root2', 'L0_gnn_b2']


def kernel(**inputs):
    import numpy as _np
    import concourse.bacc as _bacc
    from concourse import mybir as _mybir
    from concourse.bass_utils import run_bass_kernel_spmd as _run

    nc = _bacc.Bacc("TRN2", target_bir_lowering=False, num_devices=1)
    arrays, args = {}, []
    for name in _INS:
        a = _np.ascontiguousarray(inputs[name])
        arrays[f"in_{name}_dram"] = a
        args.append(nc.dram_tensor(f"in_{name}_dram", a.shape, _mybir.dt.from_np(a.dtype), kind="ExternalInput").ap())
    out = nc.dram_tensor("out_dram", inputs["x"].shape, _mybir.dt.float32, kind="ExternalOutput").ap()
    graph_block_kernel(nc, *args, out)
    r = _run(nc, [arrays], core_ids=[0])
    return r.results[0]["out_dram"]
```

```python
from contextlib import ExitStack

import concourse.bass as bass
from concourse import mybir

F32 = mybir.dt.float32
F32R = mybir.dt.float32r
BF16 = mybir.dt.bfloat16
I32 = mybir.dt.int32
ALU = mybir.AluOpType
ACT = mybir.ActivationFunctionType

P = 128
EPS = 1e-5
UNROLL = 2


class Batch:

    def __init__(self, step0, pairs, offset):
        self.value = step0 + offset
        self.parity = offset % 2
        self.earlier = pairs + offset // 2


def graph_block_kernel(nc, x, adj, w_rel1, w_root1, b1, w_rel2, w_root2, b2, out):
    BATCHES, N, D = x.shape
    K = N // P
    HALF = K // 2
    FIRST, LAST = -2, BATCHES + 1
    assert D == P and N == K * P and K % 2 == 0 and BATCHES % 2 == 0
    LOOP_FIRST = 2
    PAIRS = (BATCHES - 2 - LOOP_FIRST) // UNROLL

    WEIGHT_LOADS = 3

    X_CHUNKS = [(0, 1), (1, 2), (2, LOOP_FIRST + 2), (LOOP_FIRST + 2, BATCHES)]

    adj_rows = adj.rearrange("b (k p) j -> b p k j", p=P)
    out_rows = out.rearrange("b (k p) d -> b p k d", p=P)

    with ExitStack() as ctx:
        def sb(name, shape, dt):
            return ctx.enter_context(nc.sbuf_tensor(name, shape, dt))

        def psum(name, shape, dt):
            return ctx.enter_context(nc.psum_tensor(name, shape, dt))

        def sem(name):
            return ctx.enter_context(nc.semaphore(name))

        x_all = sb("x_all", [P, BATCHES * K, D], F32)
        adj_in = [sb(f"adj_in{i}", [P, K, N], I32) for i in range(2)]
        mask = [sb(f"mask{i}", [P, K, N], F32R) for i in range(2)]
        EMPTY_REL, REL, ROOT = 0, 1, 2
        weights = sb("weights", [P, 2, 3, D], F32)
        weights_hi = sb("weights_hi", [P, 2, 2, D], F32R)
        weights_lo = sb("weights_lo", [P, 2, 2, D], F32R)
        exp_of_zero = sb("exp_of_zero", [P, 1], F32)
        bias_in = sb("bias_in", [P, 2], F32)
        bias = sb("bias", [P, 2], F32)
        zeros = sb("zeros", [P, 1], F32)
        ones = sb("ones", [P, 1], BF16)
        ident = sb("ident", [P, P], F32)
        minus_half = sb("minus_half", [P, K], F32)
        minus_one = sb("minus_one", [P, K], F32)
        eps = sb("eps", [P, K], F32)

        block_stats = sb("block_stats", [P, K, 6], F32)
        mean_var = sb("mean_var", [P, K, 2], F32)
        var_eps = sb("var_eps", [P, K], F32)
        neg_mean = sb("neg_mean", [P, K], F32)
        rstd = sb("rstd", [P, K], F32)
        shift = sb("shift", [P, K], F32)
        h0 = sb("h0", [P, K, D], F32)
        h0_hi = sb("h0_hi", [P, K, D], F32R)
        h0_lo = sb("h0_lo", [P, K, D], F32R)
        h0T_hi = sb("h0T_hi", [P, N], F32R)
        h0T_lo = sb("h0T_lo", [P, N], F32R)
        h1_hi = sb("h1_hi", [P, K, D], F32R)
        h1_lo = sb("h1_lo", [P, K, D], F32R)
        h1T = sb("h1T", [P, N], F32)
        h1T_hi = sb("h1T_hi", [P, N], F32R)
        h1T_lo = sb("h1T_lo", [P, N], F32R)
        h2T = sb("h2T", [P, N], F32)
        expT = [sb(f"expT_l{i}", [P, N], F32) for i in range(2)]
        nT = [sb(f"nT_l{i}", [P, N], F32) for i in range(2)]
        nT_hi = [sb(f"nT_hi_l{i}", [P, N], F32R) for i in range(2)]
        nT_lo = [sb(f"nT_lo_l{i}", [P, N], F32R) for i in range(2)]
        deg = sb("deg", [P, K], F32)
        rdeg = sb("rdeg", [P, K], F32)
        rdeg_row = [sb(f"rdeg_row{i}", [P, N], F32) for i in range(2)]
        out_sb = [sb(f"out_sb{i}", [P, K, D], F32) for i in range(2)]

        agg_ps = [psum(f"agg_ps_l{i}", [P, N], F32) for i in range(2)]
        v_ps = [psum(f"v_ps_l{i}", [P, N], F32) for i in range(2)]
        h0T_ps = psum("h0T_ps", [P, N], F32)
        h1_ps = psum("h1_ps", [P, K, D], F32)
        h2_ps = psum("h2_ps", [P, K, D], F32)
        deg_ps = psum("deg_ps", [P, N], F32)

        x_loaded = [sem(f"x_loaded{i}") for i in range(len(X_CHUNKS))]
        adj_loaded = [sem(f"adj_loaded{i}") for i in range(2)]
        out_stored = [sem(f"out_stored{i}") for i in range(2)]
        weights_loaded = [sem(f"weights_loaded_l{i}") for i in range(2)]
        constants_set = sem("constants_set")
        rstd_prep = sem("rstd_prep")
        rstd_done = sem("rstd_done")
        h0_lo_done = sem("h0_lo_done")
        h1T_lo_done = sem("h1T_lo_done")
        n_lo_done = [sem(f"n_lo_done_l{i}") for i in range(2)]
        weights_lo_done = sem("weights_lo_done")
        h0_done = sem("h0_done")
        h0_hi_done = sem("h0_hi_done")
        h0T_hi_done = sem("h0T_hi_done")
        h1T_hi_done = sem("h1T_hi_done")
        n_hi_done = [sem(f"n_hi_done_l{i}") for i in range(2)]
        weights_hi_done = sem("weights_hi_done")
        h1_hi_done = sem("h1_hi_done")
        rdeg_row_done = sem("rdeg_row_done")
        exp_done = [sem(f"exp_done_l{i}") for i in range(2)]
        mask_done = sem("mask_done")
        block_stats_done = sem("block_stats_done")
        stats_done = sem("stats_done")
        deg_done = sem("deg_done")
        rdeg_done = sem("rdeg_done")
        n_done = [sem(f"n_done_l{i}") for i in range(2)]
        expm1_done = [sem(f"expm1_done_l{i}") for i in range(2)]
        h_done = [sem(f"h_done_l{i}") for i in range(2)]
        h1_lo_done = sem("h1_lo_done")
        h0T_lo_done = sem("h0T_lo_done")
        bias_done = sem("bias_done")
        out_done = sem("out_done")
        empty_relation_done = sem("empty_relation_done")
        agg_done = [sem(f"agg_done_l{i}") for i in range(2)]
        mask_half_used = sem("mask_half_used")
        linear_done = [sem(f"linear_done_l{i}") for i in range(2)]
        deg_summed = sem("deg_summed")
        h0_transposed = sem("h0_transposed")
        h1_transposed = sem("h1_transposed")
        h2_transposed = sem("h2_transposed")
        rdeg_spread = sem("rdeg_spread")

        def exists(batch):
            return not isinstance(batch.value, int) or 0 <= batch.value < BATCHES

        def wait(eng, semaphore, count):
            if not isinstance(count, int) or count > 0:
                eng.wait_ge(semaphore, count)

        def run_steps(eng, step, before={}):
            def peeled(s):
                step(lambda k: Batch(s - s % 2, (s - s % 2) // 2, s % 2 + k))

            for s in range(FIRST, LOOP_FIRST + 1):
                if s in before:
                    before[s]()
                if s < LOOP_FIRST:
                    peeled(s)
            with eng.Fori(0, PAIRS) as pair:
                for u in range(UNROLL):
                    step(lambda k, u=u: Batch(2 * pair, pair, LOOP_FIRST + u + k))
            for s in range(LOOP_FIRST + UNROLL * PAIRS, LAST + 1):
                peeled(s)

        def x_block(b, k):
            return x_all[:, bass.ds(b.value * K + k, 1), :]

        block = ctx.enter_context(nc.Block())

        @block.sync
        def _(sp):
            def load_x(chunk):
                first, last = X_CHUNKS[chunk]
                sp.dma_start(x_all[:, first * K:last * K, :],
                             x[first:last, :, :].rearrange("b (k p) d -> p (b k) d", p=P)
                             ).then_inc(x_loaded[chunk], 16)

            def load_adj(b):
                wait(sp, mask_done, b.value - 1)
                sp.dma_start(adj_in[b.parity][:], adj_rows[bass.ds(b.value, 1), :, :, :].rearrange("b p k j -> p (b k) j")
                             ).then_inc(adj_loaded[b.parity], 16)

            def store(b):
                wait(sp, out_done, b.value + 1)
                sp.dma_start(out_rows[bass.ds(b.value, 1), :, :, :].rearrange("b p k d -> p (b k) d"), out_sb[b.parity][:]
                             ).then_inc(out_stored[b.parity], 16)

            def step(at):
                if exists(at(2)):
                    load_adj(at(2))
                if exists(at(-2)):
                    store(at(-2))

            run_steps(sp, step, {-2: lambda: load_x(0), -1: lambda: load_x(1), 0: lambda: load_x(2),
                                 1: lambda: load_x(3)})
            for stored in out_stored:
                sp.wait_ge(stored, 16 * BATCHES // 2)

        @block.tensor
        def _(pe):
            def multiply_empty_relation(layer):
                pe.wait_ge(weights_loaded[layer], 16 * WEIGHT_LOADS)
                pe.wait_ge(constants_set, 1)
                nc.tensor.matmul(v_ps[1][:, layer:layer + 1], weights[:, layer, EMPTY_REL, :], zeros[:],
                                 start=True, stop=True).then_inc(empty_relation_done, 1)

            def aggregate_hi(layer, b, h_hi, h_hi_done):
                wait(pe, n_done[layer], b.value)
                pe.wait_ge(h_hi_done, b.value + 1)
                for k in range(K):
                    nc.tensor.matmul(agg_ps[layer][:], h_hi[:, k, :], mask[b.parity][:, k, :],
                                     start=(k == 0), stop=False)

            def aggregate_lo(layer, b, h_lo, h_lo_done):
                pe.wait_ge(h_lo_done, b.value + 1)
                for k in range(K):
                    mm = nc.tensor.matmul(agg_ps[layer][:], h_lo[:, k, :], mask[b.parity][:, k, :],
                                          start=False, stop=(k == K - 1))
                    if layer == 1 and k == HALF - 1:
                        mm.then_inc(mask_half_used, 1)
                mm.then_inc(agg_done[layer], 1)

            def times_hi(layer, which, hT_hi, hT_hi_done, b):
                if isinstance(b.value, int) and b.value == 0:
                    pe.wait_ge(weights_lo_done, layer + 1)
                pe.wait_ge(hT_hi_done, b.value + 1)
                for w in (weights_hi, weights_lo):
                    nc.tensor.matmul(v_ps[layer][:], w[:, layer, which - REL, :], hT_hi[:],
                                     start=(which == ROOT and w is weights_hi), stop=False)

            def times_lo(layer, which, hT_lo, hT_lo_done, b):
                pe.wait_ge(hT_lo_done, b.value + 1)
                return nc.tensor.matmul(v_ps[layer][:], weights_hi[:, layer, which - REL, :], hT_lo[:],
                                        start=False, stop=(which == REL))

            def root_hi(layer, b, hT_hi, hT_hi_done):
                wait(pe, h_done[layer], b.value)
                times_hi(layer, ROOT, hT_hi, hT_hi_done, b)

            def root_lo(layer, b, hT_lo, hT_lo_done):
                times_lo(layer, ROOT, hT_lo, hT_lo_done, b)

            def rel_hi(layer, b):
                times_hi(layer, REL, nT_hi[layer], n_hi_done[layer], b)

            def rel_lo(layer, b):
                times_lo(layer, REL, nT_lo[layer], n_lo_done[layer], b).then_inc(linear_done[layer], 1)

            def sum_degrees(b):
                pe.wait_ge(mask_done, b.value + 1)
                pe.wait_ge(constants_set, 1)
                wait(pe, rdeg_row_done, b.value)
                halves = mask[b.parity][:].bitcast(BF16).rearrange("p k (j t) -> p k j t", t=2)
                for j in range(K):
                    for k in range(K):
                        mm = nc.tensor.matmul(deg_ps[:, j:j + 1], halves[:, k, j * P:(j + 1) * P, 1], ones[:],
                                              start=(k == 0), stop=(k == K - 1))
                mm.then_inc(deg_summed, 1)

            def spread_rdeg(b):
                pe.wait_ge(rdeg_done, b.value + 1)
                for j in range(K):
                    mm = nc.tensor.transpose(deg_ps[:, j * P:(j + 1) * P],
                                             rdeg[:, j:j + 1].to_broadcast([P, P]), ident[:])
                mm.then_inc(rdeg_spread, 1)

            def transpose_h0(b):
                pe.wait_ge(h0_done, b.value + 1)
                wait(pe, h0T_lo_done, b.value)
                for k in range(K):
                    mm = nc.tensor.transpose(h0T_ps[:, k * P:(k + 1) * P], h0[:, k, :], ident[:])
                mm.then_inc(h0_transposed, 1)

            def transpose_h1(b):
                pe.wait_ge(h_done[0], b.value + 1)
                wait(pe, h1_lo_done, b.value)
                for k in range(K):
                    mm = nc.tensor.transpose(h1_ps[:, k, :], h1T[:, k * P:(k + 1) * P], ident[:])
                mm.then_inc(h1_transposed, 1)

            def transpose_h2(b):
                pe.wait_ge(h_done[1], b.value + 1)
                wait(pe, out_done, b.value)
                for k in range(K):
                    mm = nc.tensor.transpose(h2_ps[:, k, :], h2T[:, k * P:(k + 1) * P], ident[:])
                mm.then_inc(h2_transposed, 1)

            def step(at):
                if exists(at(-2)):
                    rel_hi(1, at(-2))
                if exists(at(0)):
                    root_hi(0, at(0), h0T_hi, h0T_hi_done)
                if exists(at(-2)):
                    rel_lo(1, at(-2))
                if exists(at(0)):
                    root_lo(0, at(0), h0T_lo, h0T_lo_done)
                if exists(at(-1)):
                    aggregate_hi(1, at(-1), h1_hi, h1_hi_done)
                    aggregate_lo(1, at(-1), h1_lo, h1_lo_done)
                if exists(at(0)):
                    rel_hi(0, at(0))
                    rel_lo(0, at(0))
                if exists(at(-1)):
                    root_hi(1, at(-1), h1T_hi, h1T_hi_done)
                if exists(at(1)):
                    transpose_h0(at(1))
                if exists(at(-2)):
                    transpose_h2(at(-2))
                if exists(at(1)):
                    sum_degrees(at(1))
                    aggregate_hi(0, at(1), h0_hi, h0_hi_done)
                    spread_rdeg(at(1))
                if exists(at(-1)):
                    root_lo(1, at(-1), h1T_lo, h1T_lo_done)
                if exists(at(1)):
                    aggregate_lo(0, at(1), h0_lo, h0_lo_done)
                if exists(at(0)):
                    transpose_h1(at(0))

            run_steps(pe, step, {0: lambda: multiply_empty_relation(0), 1: lambda: multiply_empty_relation(1)})

        @block.scalar
        def _(act):
            for layer, (rel, root, b) in enumerate(((w_rel1, w_root1, b1), (w_rel2, w_root2, b2))):
                if layer == 1:
                    act.wait_ge(constants_set, 1)
                    nc.scalar.activation(exp_of_zero[:], zeros[:], ACT.Exp)
                act.dma_start(weights[:, layer, EMPTY_REL:REL + 1, :], rel.rearrange("r d e -> d r e")
                              ).then_inc(weights_loaded[layer], 16)
                act.dma_start(weights[:, layer, ROOT, :], root).then_inc(weights_loaded[layer], 16)
                act.dma_start(bias_in[:, layer:layer + 1], b.rearrange("(p a) -> p a", a=1)
                              ).then_inc(weights_loaded[layer], 16)

            def round_h1(b):
                act.wait_ge(h1_transposed, b.value + 1)
                wait(act, agg_done[1], b.value)
                nc.scalar.activation(h1_hi[:], h1_ps[:], ACT.Copy).then_inc(h1_hi_done, 1)

            def copy_rdeg(b):
                act.wait_ge(rdeg_spread, b.value + 1)
                wait(act, n_done[1], b.value - 1)
                nc.scalar.activation(rdeg_row[b.parity][:], deg_ps[:], ACT.Copy).then_inc(rdeg_row_done, 1)

            def normalise(b):
                act.wait_ge(rstd_done, b.value + 1)
                wait(act, h0_transposed, b.value)
                wait(act, h0_lo_done, b.value)
                for k in range(K):
                    a = nc.scalar.activation(h0[:, k:k + 1, :], x_block(b, k), ACT.Relu,
                                             bias=shift[:, k:k + 1], scale=rstd[:, k:k + 1])
                a.then_inc(h0_done, 1)

            def round_h0(b):
                act.wait_ge(h0_done, b.value + 1)
                wait(act, agg_done[0], b.value)
                nc.scalar.activation(h0_hi[:], h0[:], ACT.Copy).then_inc(h0_hi_done, 1)

            def round_h0T(b):
                act.wait_ge(h0_transposed, b.value + 1)
                wait(act, linear_done[0], b.value)
                nc.scalar.activation(h0T_hi[:], h0T_ps[:], ACT.Copy).then_inc(h0T_hi_done, 1)

            def round_h1T(b):
                act.wait_ge(h_done[0], b.value + 1)
                wait(act, linear_done[1], b.value)
                nc.scalar.activation(h1T_hi[:], h1T[:], ACT.Copy).then_inc(h1T_hi_done, 1)

            def round_n(layer, b):
                act.wait_ge(n_done[layer], b.value + 1)
                wait(act, linear_done[layer], b.value)
                nc.scalar.activation(nT_hi[layer][:], nT[layer][:], ACT.Copy).then_inc(n_hi_done[layer], 1)

            def exp(layer, b):
                if isinstance(b.value, int) and b.value == 0:
                    act.wait_ge(bias_done, layer + 1)
                act.wait_ge(linear_done[layer], b.value + 1)
                wait(act, h_done[layer], b.value)
                nc.scalar.activation(expT[layer][:], v_ps[layer][:], ACT.Exp, bias=bias[:, layer:layer + 1]
                                     ).then_inc(exp_done[layer], 1)

            def step(at):
                if exists(at(-2)):
                    round_h1T(at(-2))
                if exists(at(0)):
                    normalise(at(0))
                    round_h0(at(0))
                if exists(at(-1)):
                    exp(0, at(-1))
                if exists(at(0)):
                    round_h0T(at(0))
                if exists(at(-2)):
                    round_n(1, at(-2))
                if exists(at(0)):
                    copy_rdeg(at(0))
                if exists(at(-1)):
                    round_h1(at(-1))
                if exists(at(0)):
                    round_n(0, at(0))
                if exists(at(-2)):
                    exp(1, at(-2))

            def round_weights(layer):
                act.wait_ge(weights_loaded[layer], 16 * WEIGHT_LOADS)
                nc.scalar.activation(weights_hi[:, layer, :, :], weights[:, layer, REL:ROOT + 1, :], ACT.Copy
                                     ).then_inc(weights_hi_done, 1)

            run_steps(act, step, {0: lambda: round_weights(0), 1: lambda: round_weights(1)})

        @block.vector
        def _(dve):
            def add_bias(layer):
                dve.wait_ge(empty_relation_done, layer + 1)
                dve.wait_ge(weights_loaded[layer], 16 * WEIGHT_LOADS)
                nc.vector.tensor_tensor(bias[:, layer:layer + 1], v_ps[1][:, layer:layer + 1],
                                        bias_in[:, layer:layer + 1], ALU.add).then_inc(bias_done, 1)

            def rest_h1(b):
                dve.wait_ge(h1_hi_done, b.value + 1)
                wait(dve, agg_done[1], b.value)
                nc.vector.tensor_tensor(h1_lo[:], h1_ps[:], h1_hi[:].bitcast(F32), ALU.subtract
                                        ).then_inc(h1_lo_done, 1)

            def divide_by_degree(layer, b):
                dve.wait_ge(agg_done[layer], b.value + 1)
                dve.wait_ge(rdeg_row_done, b.value + 1)
                wait(dve, n_lo_done[layer], b.value)
                nc.vector.tensor_tensor(nT[layer][:], agg_ps[layer][:], rdeg_row[b.parity][:], ALU.mult
                                        ).then_inc(n_done[layer], 1)

            def rest_h0T(b):
                dve.wait_ge(h0T_hi_done, b.value + 1)
                wait(dve, linear_done[0], b.value)
                nc.vector.tensor_tensor(h0T_lo[:], h0T_ps[:], h0T_hi[:].bitcast(F32), ALU.subtract
                                        ).then_inc(h0T_lo_done, 1)

            def make_mask(b, half):
                ks = slice(half * HALF, (half + 1) * HALF)
                if half == 0:
                    dve.wait_ge(adj_loaded[b.parity], 16 * (b.earlier + 1))
                    wait(dve, mask_half_used, b.value - 1)
                else:
                    wait(dve, agg_done[1], b.value - 1)
                ts = nc.vector.tensor_scalar(mask[b.parity][:, ks, :], adj_in[b.parity][:, ks, :],
                                             1.0, None, ALU.is_equal)
                if half == 1:
                    ts.then_inc(mask_done, 1)

            def statistics(b):
                if isinstance(b.value, int):
                    for chunk, (first, _) in enumerate(X_CHUNKS):
                        if b.value == first:
                            dve.wait_ge(x_loaded[chunk], 16)
                wait(dve, stats_done, b.value)
                for k in range(K):
                    bn = nc.vector.bn_stats(block_stats[:, k, :], x_block(b, k))
                bn.then_inc(block_stats_done, 1)

            def await_statistics(b):
                dve.wait_ge(block_stats_done, b.value + 1)
                wait(dve, rstd_done, b.value)

            def mean_and_variance(b):
                for k in range(K):
                    bn = nc.vector.bn_aggr(mean_var[:, k, :], block_stats[:, k, :])
                bn.then_inc(stats_done, 1)

            def expm1(layer, b):
                dve.wait_ge(exp_done[layer], b.value + 1)
                nc.vector.tensor_scalar(expT[layer][:], expT[layer][:], -1.0, 0.0, ALU.add, ALU.min
                                        ).then_inc(expm1_done[layer], 1)

            def elu(layer, b, hT):
                dve.wait_ge(expm1_done[layer], b.value + 1)
                if layer == 0:
                    wait(dve, h1_transposed, b.value)
                    wait(dve, h1T_lo_done, b.value)
                else:
                    wait(dve, h2_transposed, b.value)
                nc.vector.scalar_tensor_tensor(hT[:], v_ps[layer][:], bias[:, layer:layer + 1],
                                               expT[layer][:], ALU.add, ALU.max).then_inc(h_done[layer], 1)

            def clamp_degree(b):
                dve.wait_ge(deg_summed, b.value + 1)
                nc.vector.tensor_scalar(deg[:], deg_ps[:, 0:K], 1.0, None, ALU.max).then_inc(deg_done, 1)

            def invert_degree(b):
                dve.wait_ge(deg_done, b.value + 1)
                wait(dve, rdeg_spread, b.value)
                nc.vector.reciprocal(rdeg[:], deg[:]).then_inc(rdeg_done, 1)

            def add_x(b):
                dve.wait_ge(h2_transposed, b.value + 1)
                wait(dve, out_stored[b.parity], 16 * b.earlier)
                nc.vector.tensor_tensor(out_sb[b.parity][:], h2_ps[:], x_all[:, bass.ds(b.value * K, K), :],
                                        ALU.add).then_inc(out_done, 1)

            def step(at):
                if exists(at(0)):
                    divide_by_degree(0, at(0))
                if exists(at(-1)):
                    rest_h1(at(-1))
                if exists(at(2)):
                    statistics(at(2))
                if exists(at(-2)):
                    expm1(1, at(-2))
                    elu(1, at(-2), h2T)
                if exists(at(1)):
                    make_mask(at(1), 0)
                if exists(at(2)):
                    await_statistics(at(2))
                if exists(at(1)):
                    make_mask(at(1), 1)
                if exists(at(2)):
                    mean_and_variance(at(2))
                if exists(at(-1)):
                    divide_by_degree(1, at(-1))
                if exists(at(1)):
                    clamp_degree(at(1))
                if exists(at(0)):
                    expm1(0, at(0))
                if exists(at(1)):
                    invert_degree(at(1))
                    rest_h0T(at(1))
                if exists(at(0)):
                    elu(0, at(0), h1T)
                if exists(at(-2)):
                    add_x(at(-2))

            def await_rest_of_x():
                dve.wait_ge(x_loaded[-1], 16)

            run_steps(dve, step, {0: lambda: add_bias(0), 1: lambda: add_bias(1), LOOP_FIRST: await_rest_of_x})

        @block.gpsimd
        def _(pool):
            nc.gpsimd.memset(ones[:], 1.0)
            nc.gpsimd.memset(minus_half[:], -0.5)
            nc.gpsimd.memset(minus_one[:], -1.0)
            nc.gpsimd.memset(eps[:], EPS)
            nc.gpsimd.memset(zeros[:], 0.0)
            nc.gpsimd.memset(ident[:], 0.0).then_inc(rstd_prep, 1)
            pool.wait_ge(rstd_prep, 1)
            nc.gpsimd.affine_select(out=ident[:], in_=ident[:], compare_op=ALU.not_equal, fill=1.0, base=0,
                                    pattern=[[-1, P]], channel_multiplier=1).then_inc(constants_set, 1)

            def inverse_deviation(b):
                pool.wait_ge(stats_done, b.value + 1)
                wait(pool, h0_done, b.value)
                nc.gpsimd.tensor_tensor(var_eps[:], mean_var[:, :, 1], eps[:], ALU.add)
                nc.gpsimd.tensor_tensor(neg_mean[:], mean_var[:, :, 0], minus_one[:], ALU.mult
                                        ).then_inc(rstd_prep, 1)
                pool.wait_ge(rstd_prep, 2 * b.value + 2)
                nc.gpsimd.tensor_tensor(rstd[:], var_eps[:], minus_half[:], ALU.pow).then_inc(rstd_prep, 1)
                pool.wait_ge(rstd_prep, 2 * b.value + 3)
                nc.gpsimd.tensor_tensor(shift[:], neg_mean[:], rstd[:], ALU.mult).then_inc(rstd_done, 1)

            def rest_h0(b):
                pool.wait_ge(h0_hi_done, b.value + 1)
                wait(pool, agg_done[0], b.value)
                nc.gpsimd.tensor_tensor(h0_lo[:], h0[:], h0_hi[:].bitcast(F32), ALU.subtract
                                        ).then_inc(h0_lo_done, 1)

            def rest_h1T(b):
                pool.wait_ge(h1T_hi_done, b.value + 1)
                wait(pool, linear_done[1], b.value)
                nc.gpsimd.tensor_tensor(h1T_lo[:], h1T[:], h1T_hi[:].bitcast(F32), ALU.subtract
                                        ).then_inc(h1T_lo_done, 1)

            def rest_n(layer, b):
                pool.wait_ge(n_hi_done[layer], b.value + 1)
                wait(pool, linear_done[layer], b.value)
                nc.gpsimd.tensor_tensor(nT_lo[layer][:], nT[layer][:], nT_hi[layer][:].bitcast(F32), ALU.subtract
                                        ).then_inc(n_lo_done[layer], 1)

            def step(at):
                if exists(at(1)):
                    inverse_deviation(at(1))
                if exists(at(0)):
                    rest_n(0, at(0))
                if exists(at(-1)):
                    rest_h1T(at(-1))
                if exists(at(1)):
                    rest_h0(at(1))
                if exists(at(-1)):
                    rest_n(1, at(-1))

            def rest_weights(layer):
                pool.wait_ge(weights_hi_done, layer + 1)
                nc.gpsimd.tensor_tensor(weights_lo[:, layer, :, :], weights[:, layer, REL:ROOT + 1, :],
                                        weights_hi[:, layer, :, :].bitcast(F32), ALU.subtract
                                        ).then_inc(weights_lo_done, 1)

            run_steps(pool, step, {0: lambda: rest_weights(0), 1: lambda: rest_weights(1)})


_INS = ['x', 'adj', 'L0_gnn_w_rel1', 'L0_gnn_w_root1', 'L0_gnn_b1', 'L0_gnn_w_rel2', 'L0_gnn_w_root2', 'L0_gnn_b2']


def kernel(**inputs):
    import numpy as _np
    import concourse.bacc as _bacc
    from concourse import mybir as _mybir
    from concourse.bass_utils import run_bass_kernel_spmd as _run

    nc = _bacc.Bacc("TRN2", target_bir_lowering=False, num_devices=1)
    arrays, args = {}, []
    for name in _INS:
        a = _np.ascontiguousarray(inputs[name])
        arrays[f"in_{name}_dram"] = a
        args.append(nc.dram_tensor(f"in_{name}_dram", a.shape, _mybir.dt.from_np(a.dtype), kind="ExternalInput").ap())
    out = nc.dram_tensor("out_dram", inputs["x"].shape, _mybir.dt.float32, kind="ExternalOutput").ap()
    graph_block_kernel(nc, *args, out)
    r = _run(nc, [arrays], core_ids=[0])
    return r.results[0]["out_dram"]
```
